# Optimizing a Trainium2 kernel written in Bass

```python
import numpy as np
import jax
import jax.numpy as jnp

def _softmax(x, axis=-1):
    return jax.nn.softmax(x, axis=axis)

def _gelu(x):
    return jax.nn.gelu(x, approximate=True)

def _silu(x):
    return jax.nn.silu(x)

def _sigmoid(x):
    return jax.nn.sigmoid(x)

def _layernorm(x, axis=-1, eps=1e-05):
    m = jnp.mean(x, axis=axis, keepdims=True)
    v = jnp.var(x, axis=axis, keepdims=True)
    return (x - m) / jnp.sqrt(v + eps)

def _scatter_add(tgt, idx, src, axis=0):
    return tgt.at[idx].add(src)

def _segment_sum(src, seg, n):
    return jax.ops.segment_sum(src, seg, n)
kernel_name = 'mk_gps_d1_gnn_r8_11a605'

def setup_inputs(seed: int=0):
    np.random.seed(seed)
    _w = jnp.asarray

    def _rec_inputs():
        import jax
        import jax.numpy as jnp
        _gk = jax.random.key(seed)
        x = -0.0003713 + 1 * jax.random.normal(jax.random.fold_in(_gk, 1), (6250, 256), jnp.float32)
        _s = jax.random.randint(jax.random.fold_in(_gk, 2), (50000,), 0, 6250, jnp.int32)
        _d = jax.random.randint(jax.random.fold_in(_gk, 3), (50000,), 0, 6250, jnp.int32)
        _loop = jnp.arange(6250, dtype=jnp.int32)
        src = jnp.concatenate([_s, _d, _loop])
        dst = jnp.concatenate([_d, _s, _loop])
        _o = jnp.argsort(dst, stable=True)
        src = src[_o]
        dst = dst[_o]
        edge_attr_3 = -1.09012e-05 + 0.99985 * jax.random.normal(jax.random.fold_in(_gk, 11), (106250, 3), jnp.float32)
        return (x, src, dst, edge_attr_3)
    x, src, dst, edge_attr_3 = _rec_inputs()

    def _L0_gnn_setup():
        import jax, jax.numpy as jnp
        import numpy as np
        N = 6250
        E = 50000
        IN = 256
        H = 8
        D = 32
        EF = 3
        key = jax.random.key(seed)
        ks = jax.random.split(key, 8)
        x = jax.random.normal(ks[0], (N, IN), dtype=jnp.float32)
        edge_index = jax.random.randint(ks[1], (2, E), 0, N, dtype=jnp.int64)
        edge_attr = jax.random.normal(ks[2], (E, EF), dtype=jnp.float32)
        W = jax.random.normal(ks[3], (H * D, IN), dtype=jnp.float32) * np.float32(np.sqrt(2.0 / (IN + H * D)))
        a_src = jax.random.normal(ks[4], (H, D), dtype=jnp.float32) * np.float32(np.sqrt(2.0 / (H + D)))
        a_dst = jax.random.normal(ks[5], (H, D), dtype=jnp.float32) * np.float32(np.sqrt(2.0 / (H + D)))
        edge_W = jax.random.normal(ks[6], (H * D, EF), dtype=jnp.float32) * np.float32(np.sqrt(2.0 / (EF + H * D)))
        edge_b = jnp.zeros((H * D,), dtype=jnp.float32)
        bias = jnp.zeros((H * D,), dtype=jnp.float32)
        return {'x': x, 'W': W, 'a_src': a_src, 'a_dst': a_dst, 'edge_W': edge_W, 'edge_b': edge_b, 'bias': bias, 'edge_attr': edge_attr, 'edge_index': edge_index}
    _L0_gnn_all = _L0_gnn_setup()
    _L0_gnn_in = {k: v for k, v in _L0_gnn_all.items() if k in ('W', 'a_src', 'a_dst', 'edge_W', 'edge_b', 'bias')}
    del _L0_gnn_all

    def _L0_mix_setup():
        import math
        import jax, jax.numpy as jnp
        import numpy as np
        EPS_DIV = 1e-07
        EPS_NORM = 1e-12

        def _l2_normalize(x, axis):
            n = jnp.sqrt(jnp.sum(x * x, axis=axis, keepdims=True))
            return x / jnp.maximum(n, EPS_NORM)
        key = jax.random.key(seed)
        ks = jax.random.split(key, 5)
        b, N, C = (8, 512, 256)
        x = jax.random.normal(ks[0], (b, N, C), dtype=jnp.float32)
        W_qkv = jax.random.normal(ks[1], (C, 3 * C), dtype=jnp.float32) * (1.0 / math.sqrt(C))
        b_qkv = jax.random.normal(ks[2], (3 * C,), dtype=jnp.float32) * 0.02
        W_out = jax.random.normal(ks[3], (C, C), dtype=jnp.float32) * (1.0 / math.sqrt(C))
        b_out = jax.random.normal(ks[4], (C,), dtype=jnp.float32) * 0.02
        return {'x': x, 'W_qkv': W_qkv, 'b_qkv': b_qkv, 'W_out': W_out, 'b_out': b_out}
    _L0_mix_all = _L0_mix_setup()
    _L0_mix_in = {k: v for k, v in _L0_mix_all.items() if k in ('W_qkv', 'b_qkv', 'W_out', 'b_out')}
    del _L0_mix_all

    def _L0_ffn_setup():
        import jax, jax.numpy as jnp
        import numpy as np
        TOP_K = 2
        LN_EPS = 1e-05
        key = jax.random.key(seed)
        ks = jax.random.split(key, 8)
        B, S, D, E, H = (16, 1024, 256, 8, 1024)
        x = jax.random.normal(ks[0], (B, S, D), dtype=jnp.float32)
        Wr = jax.random.normal(ks[1], (D, E), dtype=jnp.float32) * 0.1
        br = jnp.zeros((E,), dtype=jnp.float32)
        ln_g = jnp.ones((E, D), dtype=jnp.float32)
        ln_b = jnp.zeros((E, D), dtype=jnp.float32)
        W1 = jax.random.normal(ks[2], (E, D, H), dtype=jnp.float32) * (1.0 / np.sqrt(D))
        b1 = jnp.zeros((E, H), dtype=jnp.float32)
        W2 = jax.random.normal(ks[3], (E, H, D), dtype=jnp.float32) * (1.0 / np.sqrt(H))
        b2 = jnp.zeros((E, D), dtype=jnp.float32)
        return {'x': x, 'Wr': Wr, 'br': br, 'ln_g': ln_g, 'ln_b': ln_b, 'W1': W1, 'b1': b1, 'W2': W2, 'b2': b2}
    _L0_ffn_all = _L0_ffn_setup()
    _L0_ffn_in = {k: v for k, v in _L0_ffn_all.items() if k in ('Wr', 'br', 'ln_g', 'ln_b', 'W1', 'b1', 'W2', 'b2')}
    del _L0_ffn_all
    return {'x': x, 'src': src, 'dst': dst, 'edge_attr_3': edge_attr_3, 'L0_gnn_W': _L0_gnn_in['W'], 'L0_gnn_a_src': _L0_gnn_in['a_src'], 'L0_gnn_a_dst': _L0_gnn_in['a_dst'], 'L0_gnn_edge_W': _L0_gnn_in['edge_W'], 'L0_gnn_edge_b': _L0_gnn_in['edge_b'], 'L0_gnn_bias': _L0_gnn_in['bias'], 'L0_mix_W_qkv': _L0_mix_in['W_qkv'], 'L0_mix_b_qkv': _L0_mix_in['b_qkv'], 'L0_mix_W_out': _L0_mix_in['W_out'], 'L0_mix_b_out': _L0_mix_in['b_out'], 'L0_ffn_Wr': _L0_ffn_in['Wr'], 'L0_ffn_br': _L0_ffn_in['br'], 'L0_ffn_ln_g': _L0_ffn_in['ln_g'], 'L0_ffn_ln_b': _L0_ffn_in['ln_b'], 'L0_ffn_W1': _L0_ffn_in['W1'], 'L0_ffn_b1': _L0_ffn_in['b1'], 'L0_ffn_W2': _L0_ffn_in['W2'], 'L0_ffn_b2': _L0_ffn_in['b2']}

def reference(x, src, dst, edge_attr_3, L0_gnn_W, L0_gnn_a_src, L0_gnn_a_dst, L0_gnn_edge_W, L0_gnn_edge_b, L0_gnn_bias, L0_mix_W_qkv, L0_mix_b_qkv, L0_mix_W_out, L0_mix_b_out, L0_ffn_Wr, L0_ffn_br, L0_ffn_ln_g, L0_ffn_ln_b, L0_ffn_W1, L0_ffn_b1, L0_ffn_W2, L0_ffn_b2):
    import jax
    import jax.numpy as jnp

    def _L0_gnn_ref(x, W, a_src, a_dst, edge_W, edge_b, bias, edge_attr, edge_index):
        import jax, jax.numpy as jnp
        import numpy as np
        N = 6250
        E = 50000
        IN = 256
        H = 8
        D = 32
        EF = 3
        n = x.shape[0]
        h = (x @ W.T).reshape(n, H, D)
        src, dst = (edge_index[0], edge_index[1])
        h_src = h[src]
        h_dst = h[dst]
        alpha = jnp.einsum('ehd,hd->eh', h_src, a_src) + jnp.einsum('ehd,hd->eh', h_dst, a_dst)
        enc = jax.nn.relu(edge_attr @ edge_W.T + edge_b).reshape(-1, H, D)
        alpha = alpha + jnp.sum(enc * h_dst, axis=-1)
        alpha = jnp.where(alpha >= 0, alpha, 0.2 * alpha)
        amax = jax.ops.segment_max(alpha, dst, num_segments=n)
        ex = jnp.exp(alpha - amax[dst])
        denom = jax.ops.segment_sum(ex, dst, num_segments=n)
        attn = ex / jnp.maximum(denom[dst], 1e-10)
        out = jax.ops.segment_sum(h_src * attn[..., None], dst, num_segments=n)
        return out.reshape(n, H * D) + bias

    def _L0_mix_ref(x, W_qkv, b_qkv, W_out, b_out):
        import math
        import jax, jax.numpy as jnp
        import numpy as np
        EPS_DIV = 1e-07
        EPS_NORM = 1e-12

        def _l2_normalize(x, axis):
            n = jnp.sqrt(jnp.sum(x * x, axis=axis, keepdims=True))
            return x / jnp.maximum(n, EPS_NORM)
        b, N, C = x.shape
        qkv = x @ W_qkv + b_qkv
        q, k, v = jnp.split(qkv, 3, axis=2)
        q = q - jnp.mean(q, axis=2, keepdims=True)
        k = k - jnp.mean(k, axis=2, keepdims=True)
        q2 = q * q
        k2 = k * k
        q2s = jnp.sum(q2, axis=2, keepdims=True)
        k2s = jnp.sum(k2, axis=2, keepdims=True)
        k2 = _l2_normalize(k2 / (k2s + EPS_DIV), axis=-2)
        q2 = _l2_normalize(q2 / (q2s + EPS_DIV), axis=-1)
        kv = jnp.einsum('bnc,bnd->bcd', k2, v)
        t2 = jnp.einsum('bnc,bcd->bnd', q2, kv) / math.sqrt(N)
        attn = v + t2
        return attn @ W_out + b_out

    def _L0_ffn_ref(x, Wr, br, ln_g, ln_b, W1, b1, W2, b2):
        import jax, jax.numpy as jnp
        import numpy as np
        TOP_K = 2
        LN_EPS = 1e-05
        B, S, D = x.shape
        N = B * S
        xt = x.reshape(N, D)
        logits = xt @ Wr + br
        probs = jax.nn.softmax(logits, axis=-1)
        top_p, top_idx = jax.lax.top_k(probs, TOP_K)
        weights = top_p / top_p.sum(axis=-1, keepdims=True)
        mu = xt.mean(axis=-1, keepdims=True)
        var = ((xt - mu) ** 2).mean(axis=-1, keepdims=True)
        xn = (xt - mu) * jax.lax.rsqrt(var + LN_EPS)
        xe = xn[None, :, :] * ln_g[:, None, :] + ln_b[:, None, :]
        h = jax.nn.gelu(jnp.einsum('end,edh->enh', xe, W1) + b1[:, None, :], approximate=False)
        y = jnp.einsum('enh,ehd->end', h, W2) + b2[:, None, :]
        y_tok = jnp.transpose(y, (1, 0, 2))
        sel = jnp.take_along_axis(y_tok, top_idx[:, :, None], axis=1)
        out = (weights[:, :, None] * sel).sum(axis=1)
        return out.reshape(B, S, D)
    edge_index = jnp.stack([src, dst])
    xn = _layernorm(x, axis=-1)
    x = x + _L0_gnn_ref(xn, L0_gnn_W, L0_gnn_a_src, L0_gnn_a_dst, L0_gnn_edge_W, L0_gnn_edge_b, L0_gnn_bias, edge_attr_3, edge_index) + _L0_mix_ref(xn[None], L0_mix_W_qkv, L0_mix_b_qkv, L0_mix_W_out, L0_mix_b_out)[0]
    x = x + _L0_ffn_ref(_layernorm(x, axis=-1)[None], L0_ffn_Wr, L0_ffn_br, L0_ffn_ln_g, L0_ffn_ln_b, L0_ffn_W1, L0_ffn_b1, L0_ffn_W2, L0_ffn_b2)[0]
    return x

_drawn_inputs = setup_inputs


def setup_inputs(seed=0):
    import zlib

    import numpy as np

    out = dict(_drawn_inputs(seed))
    spreads = {'L0_gnn_edge_b': (0.0, 0.1),
     'L0_gnn_bias': (0.0, 0.1),
     'L0_ffn_br': (0.0, 0.1),
     'L0_ffn_ln_g': (1.0, 0.2),
     'L0_ffn_ln_b': (0.0, 0.1),
     'L0_ffn_b1': (0.0, 0.1),
     'L0_ffn_b2': (0.0, 0.1)}
    factors = {}
    for name, (base, spread) in spreads.items():
        noise = np.random.default_rng([zlib.crc32(name.encode()), seed]).standard_normal(out[name].shape)
        drawn = base * np.exp(spread * noise) if base else spread * noise
        out[name] = jnp.asarray(drawn.astype(out[name].dtype))
    for name, factor in factors.items():
        out[name] = (out[name] * factor).astype(out[name].dtype)
    return out
```

```python
from contextlib import ExitStack

import numpy as np

import concourse.bass as bass
from concourse import mybir

F32 = mybir.dt.float32
I32 = mybir.dt.int32
BF16 = mybir.dt.bfloat16
ALU = mybir.AluOpType
ACT = mybir.ActivationFunctionType
AX = mybir.AxisListType

P = 128
N = 6250
C = 256
NT = -(-N // P)
NP = NT * P
LAST = N - (NT - 1) * P
HEADS, HD = 8, 32
E = 106250
EG = -(-E // P)
EP = EG * P
ROW = C + 2 * HEADS
REC = 32
SL = 8
DC = 64
X = 8
FH = 1024
FT = 256
FMAX = (2 * NP - X) // FT + X
LN_EPS = 1e-5
BIG = 1e30


class Chain:

    def __init__(self, eng, sem, per=0):
        self.eng, self.sem, self.per, self.base, self.k = eng, sem, per, 0, 0

    def tile(self, t):
        self.base, self.k = t * self.per, 0

    def end(self):
        assert self.k == self.per, self.k

    def step(self, ins):
        ins.then_inc(self.sem, 1)
        self.k += 1

    def wait(self):
        self.eng.wait_ge(self.sem, self.base + self.k)

    def run(self, ins):
        self.step(ins)
        self.wait()


def after(eng, sem, value):
    if not isinstance(value, int) or value > 0:
        eng.wait_ge(sem, value)


def gate(eng, sem, value, passed):
    after(eng, sem, value)
    eng.sem_inc(passed, 1)


def by_parity(eng, g, body):
    with eng.If(g % 2 == 0):
        body(0)
    with eng.Else():
        body(1)


def steps(eng, n, step, ring=2):
    for t in range(ring):
        step(t, t)
    groups = (n - 1) // ring
    with eng.Fori(1, groups) as i:
        for b in range(ring):
            step(ring * i + b, b)
    for t in range(ring * groups, n):
        step(t, t % ring)


def bc(ap, axis, n):
    shape = list(ap.shape)
    shape.insert(axis, n)
    return ap.unsqueeze(axis).to_broadcast(shape)


def at_tile(buf, t):
    return buf[:, bass.ds(t, 1), :].rearrange("p a c -> p (a c)")


def places(v, ch, mm, onehot, scan, small, below, total, ones, classes, pad):
    c = classes
    cnt, tot, off, row = small[:, 0, 0:c], small[:, 4, 0:c], small[:, 5, 0:c], small[:, 6, 0:c]
    ch.run(v.tensor_tensor_scan(scan[:], ones[:, 0:1].to_broadcast([P, onehot.shape[1]]), onehot[:], 0.0,
                                ALU.mult, ALU.add))
    ch.run(v.tensor_tensor_scan(row, ones[:, 0:c], cnt, 0.0, ALU.mult, ALU.add))
    ch.run(v.tensor_tensor(row, row, cnt, ALU.subtract))
    v.wait_ge(mm, 1)
    ch.run(v.tensor_copy(tot, total[:, 0:c]))
    if pad is not None:
        pad(tot)
    ch.run(v.tensor_tensor_scan(off, ones[:, 0:c], tot, 0.0, ALU.mult, ALU.add))
    ch.run(v.tensor_tensor(off, off, tot, ALU.subtract))
    ch.run(v.tensor_tensor(off, off, row, ALU.subtract))
    ch.run(v.scalar_tensor_tensor(out=off, in0=below[:, 0:c], scalar=-1.0, in1=off, op0=ALU.add, op1=ALU.add))
    s3 = scan[:].rearrange("p (c t) -> p c t", c=c)
    ch.run(v.tensor_tensor(s3, s3, bc(off, 2, onehot.shape[1] // c), ALU.add))


def gps_kernel(nc, x, dst_i, src_i, attr, wqk_in, bqk_in, wvT_in, bv_in, wout_in, bout_in, gbias_in, whT_in,
               wh_in, asd_in, erow_in, wr_in, br_in, lng_in, lnb_in, w1, b1_in, w2, b2_in,
               ident_in, tri_in, sel_in, iota_in, node_in, out):
    table = nc.dram_tensor("table", [NP, ROW], F32).ap()
    recs = nc.dram_tensor("recs", [EP, REC], BF16).ap()
    meta = nc.dram_tensor("meta", [NP, 4], I32).ap()
    aggs = nc.dram_tensor("aggs", [NP, C], F32).ap()
    xs = nc.dram_tensor("xs", [(FMAX + 2) * FT, C], F32).ap()
    ys = nc.dram_tensor("ys", [FMAX * FT, C], F32).ap()

    with ExitStack() as top:
        def sb(name, shape, dt=F32, ctx=top):
            return ctx.enter_context(nc.sbuf_tensor(name, shape, dt))

        def sem(name, ctx=top):
            return ctx.enter_context(nc.semaphore(name))

        psum = top.enter_context(nc.psum_tensor("psum", [P, 8 * 512], F32))
        bank = [psum[:, 512 * i:512 * i + 512] for i in range(8)]

        ident = sb("ident", [P, P])
        tri = sb("tri", [P, P])
        ones = sb("ones", [P, P])
        iota = sb("iota", [P, P])
        eps = sb("eps", [P, 1])
        xm = sb("xm", [P, NT, C])
        q2n = sb("q2n", [P, NT, C])
        kvo = sb("kvo", [P, 2, C])
        degs = sb("degs", [P, NT])
        metas = sb("metas", [P, NT, 4], I32)
        place_i = sb("place_i", [P, NT], I32)
        info = sb("info", [P, NT, 2], I32)
        ew = sb("ew", [P, 4, C], BF16)
        ident_bf = sb("ident_bf", [P, P], BF16)
        xplace = sb("xplace", [P, NT, 2], I32)
        xweight = sb("xweight", [P, 2, NT])
        xinfo = sb("xinfo", [P, X + 1, 2], I32)
        passed = sem("passed")

        with ExitStack() as ph:
            wqk = sb("wqk", [P, 2, 2, C], ctx=ph)
            bqk = sb("bqk", [P, 2, C], ctx=ph)
            wvT = sb("wvT", [P, 2, C], ctx=ph)
            bvc = sb("bvc", [P, 2], ctx=ph)
            bvrep = sb("bvrep", [P, 2, P], ctx=ph)
            wout = sb("wout", [P, 2, C], ctx=ph)
            bout = sb("bout", [P, C], ctx=ph)
            gbias = sb("gbias", [P, C], ctx=ph)
            whs = sb("whs", [P, 2, ROW], ctx=ph)
            wh = sb("wh", [P, 2, C], ctx=ph)
            asd = sb("asd", [P, 2, 2 * HEADS], ctx=ph)
            wmo = sb("wmo", [P, 2, C], ctx=ph)
            bvo = sb("bvo", [P, C], ctx=ph)
            bmo = sb("bmo", [P, C], ctx=ph)
            cen = sb("cen", [P, 6], ctx=ph)
            erow = sb("erow", [P, C], ctx=ph)
            esel = sb("esel", [P, 3], ctx=ph)
            epart = sb("epart", [P, 3, C], BF16, ctx=ph)
            erest = sb("erest", [P, C], ctx=ph)
            with ExitStack() as hs:
                zero_bf = sb("zero_bf", [P, 512], BF16, ctx=hs)
                iota_bf = sb("iota_bf", [P, P], BF16, ctx=hs)
                dsti = sb("dsti", [P, EG], I32, ctx=hs)
                part_i = sb("part_i", [P, EG], I32, ctx=hs)
                dlo = sb("dlo", [P, EG], ctx=hs)
                dhi = sb("dhi", [P, EG], ctx=hs)
                oh_lo = sb("oh_lo", [P, 3, P], BF16, ctx=hs)
                oh_hi = sb("oh_hi", [P, 3, NT], BF16, ctx=hs)
                deg = sb("deg", [P, NT], ctx=hs)
                small = sb("small", [P, 8, DC], ctx=hs)
                nodes = sb("nodes", [P, NT], I32, ctx=hs)
                msrc = sb("msrc", [P, NT, 5], I32, ctx=hs)
                mstage = sb("mstage", [P, 4, 5], I32, ctx=hs)
                dmax = sb("dmax", [P, NT], ctx=hs)
                onehot = sb("onehot", [P, DC * NT], ctx=hs)
                scan = sb("scan", [P, DC * NT], ctx=hs)

                ld_const, ld_w, ld_edge = (sem(s, hs) for s in ("ld_const", "ld_w", "ld_edge"))
                dve_c, pe_c, act_c, pool_c = (sem(s, hs) for s in ("t_dve", "t_pe", "t_act", "t_pool"))
                prep_ready, prep_mm, oh_lo_ready, oh_hi_ready, oh_used, hist_done, iota_ready, hi_ready = (
                    sem(s, hs) for s in ("prep_ready", "prep_mm", "oh_lo_ready", "oh_hi_ready", "oh_used",
                                         "hist_done", "iota_ready", "hi_ready"))
                deg_ready, deg_mm, cnt_ready, cnt_mm, msrc_ready, degs_ready, dmax_ready, meta_in = (
                    sem(s, hs) for s in ("deg_ready", "deg_mm", "cnt_ready", "cnt_mm", "msrc_ready",
                                         "degs_ready", "dmax_ready", "meta_in"))
                st_meta = [sem(f"st_meta{i}", hs) for i in range(4)]

                with nc.Block() as block:
                    @block.sync
                    def _(sp):
                        for dst, src in ((ident, ident_in), (tri, tri_in), (iota, iota_in), (esel, sel_in),
                                         (nodes, node_in)):
                            sp.dma_start(dst[:], src).then_inc(ld_const, 16)
                        sp.dma_start(dsti[:], dst_i).then_inc(ld_edge, 16)
                        rows = "(o p) c -> p o c"
                        for dst, src in ((wqk[:].rearrange("p o a c -> p o (a c)"), wqk_in.rearrange(rows, p=P)),
                                         (bqk[:].rearrange("p a c -> p (a c)"), bqk_in), (wvT[:], wvT_in.rearrange(rows, p=P)),
                                         (bvc[:], bv_in), (wout[:], wout_in.rearrange(rows, p=P)), (bout[:], bout_in),
                                         (gbias[:], gbias_in), (whs[:, :, 0:C], whT_in.rearrange(rows, p=P)),
                                         (wh[:], wh_in.rearrange(rows, p=P)), (asd[:], asd_in.rearrange(rows, p=P)),
                                         (erow[:], erow_in)):
                            sp.dma_start(dst, src).then_inc(ld_w, 16)
                        for j in range(4):
                            sp.wait_ge(st_meta[j], 16 * (NT // 4 + (j < NT % 4)))
                        sp.dma_start(metas[:], meta.rearrange("(t p) c -> p t c", p=P)).then_inc(meta_in, 16)

                    @block.gpsimd
                    def _(pool):
                        pool.wait_ge(msrc_ready, 1)

                        def place(t, j, n):
                            if n is not None:
                                gate(pool, st_meta[j], n, passed)
                            pool.tensor_copy(mstage[:, j, :], msrc[:, bass.ds(t, 1), :].rearrange("p a c -> p (a c)")).then_inc(pool_c, 1)
                            gate(pool, pool_c, t + 1, passed)
                            pool.indirect_dma_start(meta, bass.IndirectOffsetOnAxis(ap=mstage[:, j, 4:5], axis=0),
                                                    mstage[:, j, 0:4], None).then_inc(st_meta[j], 16)

                        for j in range(4):
                            place(j, j, None)
                        with pool.Fori(1, NT // 4) as i:
                            for j in range(4):
                                place(4 * i + j, j, 16 * i)
                        for j in range(NT % 4):
                            place(NT - NT % 4 + j, j, 16 * (NT // 4))
                        pool.wait_ge(degs_ready, 1)
                        pool.partition_all_reduce(dmax[:], degs[:], P, bass.bass_isa.ReduceOp.max).then_inc(dmax_ready, 1)

                    @block.tensor
                    def _(pe):
                        pe.wait_ge(prep_ready, 1)
                        pe.wait_ge(ld_w, 16 * 11)
                        for ic in range(2):
                            for o in range(2):
                                pe.matmul(bank[0][:, C * ic:C * ic + C], wvT[:, o, P * ic:P * ic + P], wout[:, o, :],
                                          start=(o == 0), stop=(o == 1), skip_group_check=True)
                        for o in range(2):
                            pe.matmul(bank[1][:, 0:C], bvrep[:, o, :], wout[:, o, :], start=(o == 0), stop=(o == 1),
                                      skip_group_check=True)
                        for ic in range(2):
                            for o in range(2):
                                mm = pe.matmul(bank[2][:, 16 * ic:16 * ic + 16], wh[:, o, P * ic:P * ic + P], asd[:, o, :],
                                               start=(o == 0), stop=(o == 1), skip_group_check=True)
                        mm.then_inc(prep_mm, 1)
                        pe.matmul(bank[3][:, 0:NT], zero_bf[:, 0:P], zero_bf[:, 0:NT], start=True, stop=False,
                                  skip_group_check=True)
                        with pe.Fori(0, EG // 3) as i:
                            for j in range(3):
                                g = 3 * i + j
                                pe.wait_ge(oh_hi_ready, g + 1)
                                pe.wait_ge(oh_lo_ready, g + 1)
                                pe.matmul(bank[3][:, 0:NT], oh_lo[:, j, :], oh_hi[:, j, :], start=False, stop=False,
                                          skip_group_check=True).then_inc(oh_used, 1)
                        pe.matmul(bank[3][:, 0:NT], zero_bf[:, 0:P], zero_bf[:, 0:NT], start=False, stop=True,
                                  skip_group_check=True).then_inc(hist_done, 1)
                        pe.wait_ge(deg_ready, 1)
                        pe.matmul(bank[4][:, 0:NT], tri[:], deg[:], start=True, stop=True)
                        pe.matmul(bank[5][:, 0:NT], ones[:], deg[:], start=True, stop=True).then_inc(deg_mm, 1)
                        pe.wait_ge(cnt_ready, 1)
                        pe.matmul(bank[6][:, 0:DC], tri[:], small[:, 0, :], start=True, stop=True)
                        pe.matmul(bank[7][:, 0:DC], ones[:], small[:, 0, :], start=True, stop=True).then_inc(cnt_mm, 1)

                    @block.vector
                    def _(v):
                        ch = Chain(v, dve_c)
                        v.sem_inc(oh_used, 3)
                        ch.step(v.memset(ones[:], 1.0))
                        ch.step(v.memset(eps[:], LN_EPS))
                        ch.step(v.memset(zero_bf[:], 0.0))
                        ch.run(v.memset(ew[:], 0.0))
                        v.wait_ge(ld_const, 16 * 5)
                        ch.step(v.tensor_copy(ident_bf[:], ident[:]))
                        ch.run(v.tensor_copy(iota_bf[:], iota[:]))
                        v.sem_inc(iota_ready, 1)
                        v.wait_ge(ld_edge, 16)
                        ch.run(v.tensor_scalar(part_i[:], dsti[:], 7, None, ALU.logical_shift_right))
                        ch.run(v.tensor_copy(dhi[:], part_i[:]))
                        v.sem_inc(hi_ready, 1)
                        ch.run(v.tensor_scalar(part_i[:], dsti[:], 127, None, ALU.bitwise_and))
                        ch.run(v.tensor_copy(dlo[:], part_i[:]))
                        v.wait_ge(ld_w, 16 * 11)
                        ch.step(v.tensor_reduce(cen[:, 0:4], wqk[:].rearrange("p o a c -> p (o a) c"), AX.X, ALU.add))
                        ch.run(v.tensor_reduce(cen[:, 4:6], bqk[:], AX.X, ALU.add))
                        ch.run(v.tensor_scalar(cen[:], cen[:], -1.0 / C, None, ALU.mult))
                        for o in range(2):
                            for a in range(2):
                                ch.step(v.tensor_scalar(wqk[:, o, a, :], wqk[:, o, a, :], cen[:, 2 * o + a:2 * o + a + 1], None, ALU.add))
                            ch.step(v.tensor_scalar(bqk[:, o, :], bqk[:, o, :], cen[:, 4 + o:5 + o], None, ALU.add))
                            ch.step(v.tensor_scalar(bvrep[:, o, :], ones[:], bvc[:, o:o + 1], None, ALU.mult))
                        ch.run(v.tensor_copy(epart[:, 0, :], erow[:]))
                        v.sem_inc(prep_ready, 1)
                        ch.run(v.tensor_tensor(erest[:], erow[:], epart[:, 0, :], ALU.subtract))
                        ch.run(v.tensor_copy(epart[:, 1, :], erest[:]))
                        ch.run(v.tensor_tensor(erest[:], erest[:], epart[:, 1, :], ALU.subtract))
                        ch.run(v.tensor_copy(epart[:, 2, :], erest[:]))
                        ch.run(v.tensor_scalar(erest[:], epart[:, 0, :], esel[:, 0:1], None, ALU.mult))
                        for j in (1, 2):
                            ch.run(v.scalar_tensor_tensor(out=erest[:], in0=epart[:, j, :], scalar=esel[:, j:j + 1],
                                                          in1=erest[:], op0=ALU.mult, op1=ALU.add))
                        for s in range(4):
                            ch.step(v.tensor_copy(ew[32 * s:32 * s + 32, s, :], erest[32 * s:32 * s + 32, :]))
                        v.wait_ge(prep_mm, 1)
                        ch.step(v.tensor_copy(wmo[:].rearrange("p o c -> p (o c)"), bank[0][:]))
                        ch.step(v.tensor_copy(whs[:, :, C:ROW], bank[2][:, 0:32].rearrange("p (o c) -> p o c", o=2)))
                        ch.run(v.tensor_copy(bvo[:], bank[1][:, 0:C]))
                        ch.run(v.tensor_tensor(bmo[:], bvo[:], bout[:], ALU.add))
                        ch.run(v.tensor_tensor(bmo[:], bmo[:], gbias[:], ALU.add))
                        k0 = ch.k
                        with v.Fori(0, EG // 3) as i:
                            for j in range(3):
                                g = 3 * i + j
                                v.wait_ge(oh_used, g + 1)
                                v.tensor_scalar(oh_hi[:, j, :], iota_bf[:, 0:NT], dhi[:, bass.ds(g, 1)], None,
                                                ALU.is_equal).then_inc(oh_hi_ready, 1)
                                v.tensor_scalar(oh_lo[:, j, :], iota_bf[:], dlo[:, bass.ds(g, 1)], None,
                                                ALU.is_equal).then_inc(oh_lo_ready, 1)
                        v.wait_ge(hist_done, 1)
                        ch.run(v.tensor_copy(deg[:], bank[3][:, 0:NT]))
                        v.sem_inc(deg_ready, 1)
                        cls, ptr, tmp = small[:, 1, 0:NT], small[:, 2, 0:NT], small[:, 3, 0:NT]
                        ch.run(v.tensor_scalar(cls, deg[:], float(DC - 1), None, ALU.min))
                        oh3 = onehot[:].rearrange("p (c t) -> p c t", c=DC)
                        ch.run(v.tensor_tensor(oh3, bc(iota[:, 0:DC], 2, NT), bc(cls, 1, DC), ALU.is_equal))
                        ch.run(v.tensor_reduce(small[:, 0, :], oh3, AX.X, ALU.add))
                        v.sem_inc(cnt_ready, 1)
                        v.wait_ge(deg_mm, 1)
                        ch.run(v.tensor_tensor_scan(tmp, ones[:, 0:NT], bank[5][:, 0:NT], 0.0, ALU.mult, ALU.add))
                        ch.run(v.tensor_tensor(tmp, tmp, bank[5][:, 0:NT], ALU.subtract))
                        ch.run(v.tensor_tensor(ptr, tmp, bank[4][:, 0:NT], ALU.add))
                        pos = small[:, 7, 0:NT]
                        places(v, ch, cnt_mm, onehot, scan, small, bank[6], bank[7], ones, DC, None)
                        ch.run(v.tensor_tensor(scan[:], scan[:], onehot[:], ALU.mult))
                        ch.run(v.tensor_reduce(pos, scan[:].rearrange("p (c t) -> p t c", c=DC), AX.X, ALU.add))
                        ch.step(v.tensor_copy(msrc[:, :, 0], nodes[:]))
                        ch.step(v.tensor_copy(msrc[:, :, 1], ptr))
                        ch.step(v.tensor_copy(msrc[:, :, 2], deg[:]))
                        ch.step(v.memset(msrc[:, :, 3], 0))
                        ch.step(v.tensor_copy(msrc[:, :, 4], pos))
                        ch.run(v.tensor_copy(place_i[:], pos))
                        v.sem_inc(msrc_ready, 1)
                        v.wait_ge(meta_in, 16)
                        ch.run(v.tensor_copy(degs[:], metas[:, :, 2]))
                        v.sem_inc(degs_ready, 1)
                        v.wait_ge(dmax_ready, 1)
                        ch.run(v.tensor_scalar(dmax[:], dmax[:], float(SL - 1), float(SL), ALU.add, ALU.max))
                        ch.run(v.tensor_copy(info[:, :, 1], dmax[:]))
                        ch.run(v.tensor_scalar(info[:, :, 0], info[:, :, 1], 3, None, ALU.logical_shift_right))
                        ch.run(v.tensor_copy(dmax[:], info[:, :, 0]))
                        ch.run(v.tensor_tensor_scan(tmp, ones[:, 0:NT], dmax[:], 0.0, ALU.mult, ALU.add))
                        ch.run(v.tensor_tensor(tmp, tmp, dmax[:], ALU.subtract))
                        ch.run(v.tensor_copy(info[:, :, 1], tmp))

            with ExitStack() as rc:
                RG = EG // 3
                att = sb("att", [P, EG, 3], ctx=rc)
                srci = sb("srci", [P, EG], I32, ctx=rc)
                rest = sb("rest", [P, RG, 3], ctx=rc)
                rec = sb("rec", [P, RG, REC], BF16, ctx=rc)
                ld_att, rec_split, rec_copied, st_rec, r_dve, r_act = (
                    sem(s, rc) for s in ("ld_att", "rec_split", "rec_copied", "st_rec", "r_dve", "r_act"))
                recs_v = recs.rearrange("(p g) c -> p g c", p=P)
                with nc.Block() as block:
                    @block.sync
                    def _(sp):
                        sp.dma_start(att[:], attr).then_inc(ld_att, 16)
                        sp.dma_start(srci[:], src_i).then_inc(ld_att, 16)
                        for k in range(3):
                            sp.wait_ge(rec_copied, k + 1)
                            sp.dma_start(recs_v[:, RG * k:RG * k + RG, :], rec[:]).then_inc(st_rec, 16)
                        sp.wait_ge(st_rec, 48)

                    @block.vector
                    def _(v):
                        ch = Chain(v, r_dve)
                        v.wait_ge(ld_att, 32)
                        for k in range(3):
                            g = slice(RG * k, RG * k + RG)
                            if k:
                                v.wait_ge(st_rec, 16 * k)
                            ch.run(v.tensor_copy(rec[:, :, 0:3], att[:, g, :]))
                            ch.run(v.tensor_tensor(rest[:], att[:, g, :], rec[:, :, 0:3], ALU.subtract))
                            ch.run(v.tensor_copy(rec[:, :, 3:6], rest[:]))
                            ch.run(v.tensor_tensor(rest[:], rest[:], rec[:, :, 3:6], ALU.subtract))
                            ch.run(v.tensor_copy(rec[:, :, 6:9], rest[:]))
                            v.sem_inc(rec_split, 1)
                            ch.step(v.memset(rec[:, :, 27:30], 1.0))
                            ch.run(v.tensor_copy(rec[:].bitcast(I32)[:, :, REC // 2 - 1], srci[:, g]))
                            v.sem_inc(rec_split, 1)

                    @block.scalar
                    def _(act):
                        ch = Chain(act, r_act)
                        for k in range(3):
                            act.wait_ge(rec_split, 2 * k + 1)
                            for j in (1, 2):
                                ch.run(act.copy(rec[:, :, 9 * j:9 * j + 9], rec[:, :, 0:9]))
                            act.wait_ge(rec_split, 2 * k + 2)
                            act.sem_inc(rec_copied, 1)

            with ExitStack() as nd:
                xn = sb("xn", [P, 2, C], ctx=nd)
                xT = sb("xT", [P, 2, C], ctx=nd)
                tab = sb("tab", [P, 2, ROW], ctx=nd)
                qk = sb("qk", [P, 2, 2, C], ctx=nd)
                sq = sb("sq", [P, 2, 2, C], ctx=nd)
                k2n = sb("k2n", [P, 2, C], ctx=nd)
                k4 = sb("k4", [P, 2, C], ctx=nd)
                junk = sb("junk", [P, C], ctx=nd)
                st = sb("st", [P, 2, 6], ctx=nd)
                mv = sb("mv", [P, 2, 2], ctx=nd)
                sc = sb("sc", [P, 2, 12], ctx=nd)
                gts = sb("gts", [P, 2, C], ctx=nd)
                cols = sb("cols", [P, 8], ctx=nd)
                zero = sb("zero", [P, 512], ctx=nd)
                c_ln, c_post, c_act, c_end = (sem(s, nd) for s in ("c_ln", "c_post", "c_act", "c_end"))
                ld_x, x_ready, var_ready, sd_ready, xn_ready, xt_mm, xt_ready, q_mm, h_mm, m_mm = (
                    sem(s, nd) for s in ("ld_x", "x_ready", "var_ready", "sd_ready", "xn_ready", "xt_mm",
                                         "xt_ready", "q_mm", "h_mm", "m_mm"))
                qk_ready, k2_ready, q4_ready, k2n_ready, k4_ready, g_mm, q2n_ready, m_added = (
                    sem(s, nd) for s in ("qk_ready", "k2_ready", "q4_ready", "k2n_ready", "k4_ready", "g_mm",
                                         "q2n_ready", "m_added"))
                tab_ready, zero_ready, ss_ready, rs_ready, gt_ready, kv_mm = (
                    sem(s, nd) for s in ("tab_ready", "zero_ready", "ss_ready", "rs_ready", "gt_ready", "kv_mm"))
                st_zero = sem("st_zero", nd)
                st_tab = [sem(f"st_tab{i}", nd) for i in range(2)]
                XT, QP, HP, MP, GP, CP = bank[0], bank[1], bank[2], bank[3], bank[4], bank[5]

                with nc.Block() as block:
                    @block.sync
                    def _(sp):
                        v3 = x[0:(NT - 1) * P, :].rearrange("(t p) c -> p t c", p=P)
                        for a in range(4):
                            sp.dma_start(xm[:, 12 * a:12 * a + 12, :], v3[:, 12 * a:12 * a + 12, :]).then_inc(ld_x, 16)
                        sp.wait_ge(x_ready, 1)
                        sp.dma_start(xm[0:LAST, NT - 1, :], x[(NT - 1) * P:N, :]).then_inc(ld_x, 16)

                        sp.wait_ge(zero_ready, 1)
                        sp.dma_start(xs.rearrange("(r p) c -> p r c", p=P), bc(zero[:, 0:C], 1, (FMAX + 2) * FT // P)).then_inc(st_zero, 16)
                        sp.dma_start(ys.rearrange("(r p) c -> p r c", p=P), bc(zero[:, 0:C], 1, FMAX * FT // P)).then_inc(st_zero, 16)

                        def store(t, b):
                            after(sp, tab_ready, t + 1)
                            sp.dma_start(table[bass.ds(t * P, P), :], tab[:, b, :]).then_inc(st_tab[b], 16)

                        steps(sp, NT, store)
                        sp.wait_ge(st_zero, 32)
                        sp.wait_ge(st_tab[0], 16 * 25)
                        sp.wait_ge(st_tab[1], 16 * 24)

                    @block.tensor
                    def _(pe):
                        pe.wait_ge(zero_ready, 1)
                        pe.matmul(GP[:], zero[:, 0:P], zero[:], start=True, stop=False, skip_group_check=True)
                        pe.matmul(CP[:, 0:4], zero[:, 0:P], zero[:, 0:4], start=True, stop=False, skip_group_check=True)

                        def project(t, b):
                            after(pe, xn_ready, t + 1)
                            after(pe, xt_ready, t)
                            for o in range(2):
                                mm = pe.transpose(XT[:, P * o:P * o + P], xn[:, b, P * o:P * o + P], ident[:])
                            mm.then_inc(xt_mm, 1)
                            for ps, w, width, free, done in (
                                    (QP, wqk[:].rearrange("p o a c -> p o (a c)"), 2 * C, qk_ready, q_mm),
                                    (HP, whs, ROW, tab_ready, h_mm), (MP, wmo, C, m_added, m_mm)):
                                after(pe, free, t)
                                if done is q_mm:
                                    after(pe, xt_ready, t + 1)
                                for o in range(2):
                                    mm = pe.matmul(ps[:, 0:width], xT[:, b, P * o:P * o + P], w[:, o, :],
                                                   start=(o == 0), stop=(o == 1))
                                mm.then_inc(done, 1)

                        def sums(t, b, n):
                            after(pe, k2n_ready, t + 1)
                            after(pe, k4_ready, t + 1)
                            for o in range(2):
                                pe.matmul(GP[:, C * o:C * o + C], xn[0:n, b, P * o:P * o + P], k2n[0:n, b, :],
                                          start=False, stop=False, skip_group_check=True)
                                pe.matmul(CP[:, o:o + 1], k2n[0:n, b, P * o:P * o + P], ones[0:n, 0:1],
                                          start=False, stop=False, skip_group_check=True)
                                mm = pe.matmul(CP[:, 2 + o:3 + o], k4[0:n, b, P * o:P * o + P], ones[0:n, 0:1],
                                               start=False, stop=False, skip_group_check=True)
                            mm.then_inc(g_mm, 1)

                        def step(t, b):
                            if not (isinstance(t, int) and t == NT):
                                project(t, b)
                            if not (isinstance(t, int) and t == 0):
                                sums(t - 1, 1 - b, LAST if isinstance(t, int) and t == NT else P)

                        steps(pe, NT + 1, step)
                        pe.wait_ge(gt_ready, 1)
                        for cb in range(2):
                            for o in range(2):
                                mm = pe.matmul(XT[:, C * cb:C * cb + C], gts[:, o, P * cb:P * cb + P], wmo[:, o, :],
                                               start=(o == 0), stop=(o == 1), skip_group_check=True)
                        mm.then_inc(kv_mm, 1)

                    @block.scalar
                    def _(act):
                        def first(t, b):
                            after(act, var_ready, t + 1)
                            act.activation(sc[:, b, 0:1], mv[:, b, 1:2], ACT.Sqrt, bias=eps[:, 0:1]).then_inc(sd_ready, 1)
                            after(act, m_mm, t - 1)
                            after(act, xt_mm, t + 1)
                            act.copy(xT[:, b, :], XT[:, 0:C]).then_inc(xt_ready, 1)

                        def squares(t, b):
                            after(act, qk_ready, t + 1)
                            after(act, q2n_ready, t - 1)
                            act.activation(sq[:, b, 1, :], qk[:, b, 1, :], ACT.Square, accum_out=sc[:, b, 1:2]).then_inc(k2_ready, 1)
                            act.activation(sq[:, b, 0, :], qk[:, b, 0, :], ACT.Square, accum_out=sc[:, b, 2:3]).then_inc(c_act, 1)
                            after(act, c_act, 2 * t + 1)
                            act.activation(junk[:], sq[:, b, 0, :], ACT.Square, accum_out=sc[:, b, 3:4]).then_inc(c_act, 1)
                            after(act, c_act, 2 * t + 2)
                            act.activation(sc[:, b, 4:5], sc[:, b, 3:4], ACT.Sqrt).then_inc(q4_ready, 1)
                            after(act, k2n_ready, t + 1)
                            after(act, g_mm, t - 1)
                            act.activation(k4[:, b, :], k2n[:, b, :], ACT.Square).then_inc(k4_ready, 1)

                        def step(t, b):
                            if not (isinstance(t, int) and t == NT):
                                first(t, b)
                            if not (isinstance(t, int) and t == 0):
                                squares(t - 1, 1 - b)

                        steps(act, NT + 1, step)
                        act.wait_ge(ss_ready, 1)
                        act.activation(cols[:, 6:8], cols[:, 2:4], ACT.Sqrt).then_inc(rs_ready, 1)

                    @block.vector
                    def _(v):
                        v.memset(zero[:], 0.0).then_inc(zero_ready, 1)
                        v.memset(xm[:, NT - 1, :], 0.0).then_inc(x_ready, 1)
                        v.wait_ge(ld_x, 16 * 5)
                        ln, po = Chain(v, c_ln, 2), Chain(v, c_post, 9)

                        def first(t, b):
                            ln.tile(t)
                            row = at_tile(xm, t)
                            ln.step(v.bn_stats(st[:, b, :], row))
                            gate(v, c_ln, ln.base + ln.k, passed)
                            v.bn_aggr(mv[:, b, :], st[:, b, :]).then_inc(var_ready, 1)
                            after(v, sd_ready, t + 1)
                            ln.run(v.reciprocal(sc[:, b, 5:6], sc[:, b, 0:1]))
                            after(v, g_mm, t - 1)
                            v.tensor_scalar(xn[:, b, :], row, mv[:, b, 0:1], sc[:, b, 5:6], ALU.subtract,
                                            ALU.mult).then_inc(xn_ready, 1)
                            ln.end()

                        def second(t, b):
                            po.tile(t)
                            row = at_tile(xm, t)
                            after(v, q_mm, t + 1)
                            v.tensor_tensor(qk[:, b, :, :].rearrange("p a c -> p (a c)"), QP[:],
                                            bqk[:].rearrange("p a c -> p (a c)"), ALU.add).then_inc(qk_ready, 1)
                            after(v, st_tab[b], 8 * (t - b))
                            after(v, h_mm, t + 1)
                            v.tensor_copy(tab[:, b, :], HP[:, 0:ROW]).then_inc(tab_ready, 1)
                            after(v, m_mm, t + 1)
                            po.step(v.tensor_tensor(row, row, bmo[:], ALU.add))
                            po.wait()
                            v.tensor_tensor(row, row, MP[:, 0:C], ALU.add).then_inc(m_added, 1)
                            after(v, k2_ready, t + 1)
                            po.run(v.tensor_scalar(sc[:, b, 6:7], sc[:, b, 1:2], 1e-7, None, ALU.add))
                            po.run(v.reciprocal(sc[:, b, 6:7], sc[:, b, 6:7]))
                            v.tensor_scalar(k2n[:, b, :], sq[:, b, 1, :], sc[:, b, 6:7], None, ALU.mult).then_inc(k2n_ready, 1)
                            after(v, q4_ready, t + 1)
                            po.run(v.tensor_scalar(sc[:, b, 7:8], sc[:, b, 2:3], 1e-7, None, ALU.add))
                            po.run(v.reciprocal(sc[:, b, 7:8], sc[:, b, 7:8]))
                            po.run(v.tensor_tensor(sc[:, b, 8:9], sc[:, b, 4:5], sc[:, b, 7:8], ALU.mult))
                            po.run(v.tensor_scalar(sc[:, b, 8:9], sc[:, b, 8:9], 1e-12, None, ALU.max))
                            po.run(v.reciprocal(sc[:, b, 8:9], sc[:, b, 8:9]))
                            po.run(v.tensor_tensor(sc[:, b, 9:10], sc[:, b, 7:8], sc[:, b, 8:9], ALU.mult))
                            v.tensor_scalar(at_tile(q2n, t), sq[:, b, 0, :], sc[:, b, 9:10], None, ALU.mult).then_inc(q2n_ready, 1)
                            po.end()

                        def step(t, b):
                            if not (isinstance(t, int) and t == NT):
                                first(t, b)
                            if not (isinstance(t, int) and t == 0):
                                second(t - 1, 1 - b)

                        steps(v, NT + 1, step)
                        ch = Chain(v, c_end, 0)
                        v.wait_ge(g_mm, NT)
                        ch.run(v.tensor_copy(cols[:, 0:4], CP[:, 0:4]))
                        v.sem_inc(ss_ready, 1)
                        ch.run(v.tensor_copy(gts[:].rearrange("p o c -> p (o c)"), GP[:]))
                        v.sem_inc(gt_ready, 1)
                        v.wait_ge(rs_ready, 1)
                        ch.run(v.tensor_scalar(cols[:, 4:6], cols[:, 6:8], 1e-12, float(np.sqrt(N)), ALU.max, ALU.mult))
                        ch.run(v.reciprocal(cols[:, 4:6], cols[:, 4:6]))
                        v.wait_ge(kv_mm, 1)
                        for cb in range(2):
                            ch.run(v.scalar_tensor_tensor(out=kvo[:, cb, :], in0=bvo[:], scalar=cols[:, cb:cb + 1],
                                                          in1=XT[:, C * cb:C * cb + C], op0=ALU.mult, op1=ALU.add))
                            ch.run(v.tensor_scalar(kvo[:, cb, :], kvo[:, cb, :], cols[:, 4 + cb:5 + cb], None, ALU.mult))

        with ExitStack() as ed:
            recb = sb("recb", [P, 2, SL * REC], BF16, ctx=ed)
            recT = sb("recT", [P, 2, P], BF16, ctx=ed)
            hbuf = sb("hbuf", [P, 2, SL, ROW], ctx=ed)
            hd = sb("hd", [P, 2, ROW], ctx=ed)
            nid = sb("nid", [P, 2], I32, ctx=ed)
            cur = sb("cur", [P, 1], I32, ctx=ed)
            offs = sb("offs", [P, 2], I32, ctx=ed)
            idx = sb("idx", [P, 2, SL], I32, ctx=ed)
            prod = sb("prod", [P, SL, C], ctx=ed)
            msg = sb("msg", [P, SL, C], ctx=ed)
            al = sb("al", [P, (SL + 1) * HEADS], ctx=ed)
            pr = sb("pr", [P, (SL + 1) * HEADS], ctx=ed)
            vmax = sb("vmax", [P, 2, HEADS], ctx=ed)
            run_m = sb("run_m", [P, HEADS], ctx=ed)
            run_l = sb("run_l", [P, HEADS], ctx=ed)
            run_o = sb("run_o", [P, C], ctx=ed)
            mneg = sb("mneg", [P, SL], ctx=ed)
            rem = sb("rem", [P, 1], ctx=ed)
            rl = sb("rl", [P, HEADS], ctx=ed)
            oo = sb("oo", [P, 2, C], ctx=ed)
            c_pool, c_node, c_dve, c_tile = (sem(s, ed) for s in ("c_pool", "c_node", "c_dve", "c_tile"))
            rec_free, rt_ready, enc_mm, enc_used0, enc_used1 = (
                sem(s, ed) for s in ("rec_free", "rt_ready", "enc_mm", "enc_used0", "enc_used1"))
            msg_ready, acc_mm, acc_used, al_ready, exp_ready, h_used, oo_ready, hd_used = (
                sem(s, ed) for s in ("msg_ready", "acc_mm", "acc_used", "al_ready", "exp_ready", "h_used",
                                     "oo_ready", "hd_used"))
            ld_rec = [sem(f"ld_rec{i}", ed) for i in range(2)]
            ld_h = [sem(f"ld_h{i}", ed) for i in range(2)]
            ld_hd = [sem(f"ld_hd{i}", ed) for i in range(2)]
            st_oo = [sem(f"st_oo{i}", ed) for i in range(2)]
            RT = bank[7].bitcast(BF16)
            AC = bank[6]

            def chunks_of(eng, t):
                n = eng.value_load(info[0:1, bass.ds(t, 1), 0], min_val=1, max_val=E // SL + 1)
                before = eng.value_load(info[0:1, bass.ds(t, 1), 1], min_val=0, max_val=E)
                return n, before

            def all_chunks(eng):
                n, before = chunks_of(eng, NT - 1)
                return eng.snap(n + before)

            with nc.Block() as block:
                @block.sync
                def _(sp):
                    def store(t, b):
                        after(sp, oo_ready, t + 1)
                        sp.dma_start(aggs[bass.ds(t * P, P), :], oo[:, b, :]).then_inc(st_oo[b], 16)

                    steps(sp, NT, store)
                    sp.wait_ge(st_oo[0], 16 * 25)
                    sp.wait_ge(st_oo[1], 16 * 24)

                @block.gpsimd
                def _(pool):
                    def fetch_records(b):
                        pool.indirect_dma_start(recb[:, b, :], None, recs,
                                                bass.IndirectOffsetOnAxis(ap=offs[:, b:b + 1], axis=0)).then_inc(ld_rec[b], 16)

                    pool.tensor_copy(cur[:], metas[:, 0, 1:2]).then_inc(c_node, 1)
                    pool.wait_ge(c_node, 1)
                    pool.tensor_scalar(offs[:, 0:1], cur[:], float(E), None, ALU.min).then_inc(c_node, 1)
                    pool.wait_ge(c_node, 2)
                    fetch_records(0)

                    def tile(t, tb):
                        gate(pool, hd_used, t - 1, passed) if not isinstance(t, int) or t > 1 else None
                        pool.tensor_copy(nid[:, tb:tb + 1], metas[:, bass.ds(t, 1), 0]).then_inc(c_node, 1)
                        gate(pool, c_node, t + 3, passed)
                        pool.indirect_dma_start(hd[:, tb, :], None, table,
                                                bass.IndirectOffsetOnAxis(ap=nid[:, tb:tb + 1], axis=0)).then_inc(ld_hd[tb], 16)
                        n, before = chunks_of(pool, t)
                        following = t + 1 if not isinstance(t, int) or t < NT - 1 else t
                        with pool.Fori(0, n) as c:
                            g = pool.snap(before + c)
                            gate(pool, c_pool, g * 3 + 1, passed)
                            with pool.If(c + 1 < n):
                                pool.tensor_scalar(cur[:], cur[:], float(SL), None, ALU.add).then_inc(c_pool, 1)
                            with pool.Else():
                                pool.tensor_copy(cur[:], metas[:, bass.ds(following, 1), 1]).then_inc(c_pool, 1)

                            def chunk(b):
                                gate(pool, c_pool, g * 3 + 2, passed)
                                pool.tensor_scalar(offs[:, 1 - b:2 - b], cur[:], float(E), None, ALU.min).then_inc(c_pool, 1)
                                gate(pool, c_pool, g * 3 + 3, passed)
                                gate(pool, rec_free, g + 1, passed)
                                fetch_records(1 - b)
                                gate(pool, ld_rec[b], (g - b) * 8 + 16, passed)
                                gate(pool, h_used, g + 1, passed)
                                pool.tensor_copy(idx[:, b, :], recb[:, b, :].bitcast(I32).rearrange(
                                    "p (s r) -> p s r", s=SL)[:, :, REC // 2 - 1]).then_inc(c_pool, 1)
                                gate(pool, c_pool, g * 3 + 4, passed)
                                for s in range(SL):
                                    pool.indirect_dma_start(hbuf[:, b, s, :], None, table, bass.IndirectOffsetOnAxis(
                                        ap=idx[:, b, s:s + 1], axis=0)).then_inc(ld_h[b], 16)

                            by_parity(pool, g, chunk)

                    pool.sem_inc(c_pool, 1)
                    steps(pool, NT, tile)

                @block.tensor
                def _(pe):
                    pe.sem_inc(rec_free, 1)
                    pe.sem_inc(acc_mm, 1)

                    def encode(g, b, records):
                        pe.wait_ge(ld_rec[b], records)
                        after(pe, rt_ready, g)
                        for h in range(2):
                            mm = pe.transpose(RT[:, P * h:P * h + P], recb[:, b, P * h:P * h + P], ident_bf[:])
                        mm.then_inc(rec_free, 1)
                        after(pe, rt_ready, g + 1)
                        for h in range(2):
                            after(pe, (enc_used0, enc_used1)[h], g)
                            for q in range(2):
                                mm = pe.matmul(bank[2 * h + q], recT[:, h, :],
                                               ew[:].rearrange("p s c -> p (s c)")[:, 512 * q:512 * q + 512],
                                               start=True, stop=True)
                            mm.then_inc(enc_mm, 1)

                    encode(0, 0, 16)
                    with pe.Fori(0, all_chunks(pe)) as g:
                        def chunk(b):
                            encode(g + 1, 1 - b, (g + b) * 8 + 16)
                            after(pe, acc_used, g + 1)
                            for s in range(SL):
                                if s % 4 == 0:
                                    after(pe, msg_ready, 2 * g + s // 4 + 1)
                                mm = pe.matmul(AC[:, 0:C], ident[:], msg[:, s, :], start=(s == 0), stop=(s == SL - 1))
                            mm.then_inc(acc_mm, 1)

                        by_parity(pe, g, chunk)

                @block.scalar
                def _(act):
                    act.wait_ge(rec_free, 2)
                    act.copy(recT[:].rearrange("p h e -> p (h e)"), RT[:, 0:2 * P]).then_inc(rt_ready, 1)
                    with act.Fori(0, all_chunks(act)) as g:
                        after(act, enc_mm, 2 * g + 2)
                        after(act, rec_free, g + 3)
                        act.copy(recT[:].rearrange("p h e -> p (h e)"), RT[:, 0:2 * P]).then_inc(rt_ready, 1)
                        after(act, al_ready, g + 1)
                        act.activation(pr[:], al[:], ACT.Exp).then_inc(exp_ready, 1)

                @block.vector
                def _(v):
                    ch, tl = Chain(v, c_dve, 15), Chain(v, c_tile, 6)
                    v.sem_inc(h_used, 2)
                    v.sem_inc(acc_used, 1)
                    al3 = al[:, 0:SL * HEADS].rearrange("p (s h) -> p s h", s=SL)
                    pr3 = pr[:, 0:SL * HEADS].rearrange("p (s h) -> p s h", s=SL)
                    alm, prm = al[:, SL * HEADS:], pr[:, SL * HEADS:]
                    o3 = run_o[:].rearrange("p (h d) -> p h d", h=HEADS)

                    def tile(t, tb):
                        tl.tile(t)
                        tl.step(v.memset(run_m[:], -BIG))
                        tl.step(v.memset(run_l[:], 0.0))
                        tl.step(v.memset(run_o[:], 0.0))
                        tl.run(v.tensor_copy(rem[:], degs[:, bass.ds(t, 1)]))
                        after(v, ld_hd[tb], (t - tb) * 8 + 16)
                        n, before = chunks_of(v, t)
                        with v.Fori(0, n) as c:
                            g = v.snap(before + c)

                            def chunk(b):
                                ch.tile(g)
                                for h, used in enumerate((enc_used0, enc_used1)):
                                    after(v, enc_mm, 2 * g + 1 + h)
                                    v.scalar_tensor_tensor(
                                        out=prod[:, 4 * h:4 * h + 4, :],
                                        in0=psum[:, 1024 * h:1024 * h + 1024].rearrange("p (s c) -> p s c", s=4),
                                        scalar=0.0, in1=bc(hd[:, tb, 0:C], 1, 4), op0=ALU.max, op1=ALU.mult).then_inc(used, 1)
                                after(v, enc_used1, g + 1)
                                ch.run(v.tensor_reduce(al[:, 0:SL * HEADS], prod[:].rearrange("p s (h d) -> p (s h) d", h=HEADS),
                                                       AX.X, ALU.add))
                                ch.run(v.tensor_tensor(al3, al3, bc(hd[:, tb, C + HEADS:ROW], 1, SL), ALU.add))
                                ch.step(v.tensor_scalar(mneg[:], iota[:, 0:SL], rem[:], -2.0 * BIG, ALU.is_ge, ALU.mult))
                                after(v, ld_h[b], (g - b) * (8 * SL) + 16 * SL)
                                ch.run(v.tensor_tensor(al3, al3, hbuf[:, b, :, C:C + HEADS], ALU.add))
                                ch.run(v.scalar_tensor_tensor(out=al3, in0=al3, scalar=0.2, in1=al3, op0=ALU.mult, op1=ALU.max))
                                ch.run(v.tensor_tensor(al3, al3, bc(mneg[:], 2, HEADS), ALU.add))
                                ch.step(v.tensor_scalar(rem[:], rem[:], -float(SL), None, ALU.add))
                                ch.run(v.tensor_reduce(vmax[:, 0, :], al3.rearrange("p s h -> p h s"), AX.X, ALU.max))
                                ch.run(v.tensor_tensor(vmax[:, 1, :], vmax[:, 0, :], run_m[:], ALU.max))
                                ch.step(v.tensor_tensor(al3, al3, bc(vmax[:, 1, :], 1, SL), ALU.subtract))
                                ch.run(v.tensor_tensor(alm, run_m[:], vmax[:, 1, :], ALU.subtract))
                                v.tensor_copy(run_m[:], vmax[:, 1, :]).then_inc(al_ready, 1)
                                after(v, exp_ready, g + 1)
                                after(v, acc_mm, g + 1)
                                for h in range(2):
                                    s = slice(4 * h, 4 * h + 4)
                                    v.tensor_tensor(msg[:, s, :].rearrange("p s (h d) -> p s h d", h=HEADS),
                                                    hbuf[:, b, s, 0:C].rearrange("p s (h d) -> p s h d", h=HEADS),
                                                    bc(pr3[:, s, :], 3, HD), ALU.mult).then_inc(msg_ready, 1)
                                after(v, msg_ready, 2 * g + 2)
                                v.sem_inc(h_used, 1)
                                ch.step(v.tensor_reduce(vmax[:, 0, :], pr3.rearrange("p s h -> p h s"), AX.X, ALU.add))
                                ch.run(v.tensor_tensor(run_l[:], run_l[:], prm, ALU.mult))
                                ch.step(v.tensor_tensor(run_l[:], run_l[:], vmax[:, 0, :], ALU.add))
                                ch.run(v.tensor_tensor(o3, o3, bc(prm, 2, HD), ALU.mult))
                                after(v, acc_mm, g + 2)
                                v.tensor_tensor(run_o[:], run_o[:], AC[:, 0:C], ALU.add).then_inc(acc_used, 1)
                                after(v, acc_used, g + 2)
                                v.sem_inc(passed, 1)
                                ch.end()

                            by_parity(v, g, chunk)
                        v.sem_inc(hd_used, 1)
                        tl.run(v.tensor_scalar(rl[:], run_l[:], 1e-10, None, ALU.max))
                        tl.run(v.reciprocal(rl[:], rl[:]))
                        after(v, st_oo[tb], (t - tb) * 8)
                        v.tensor_tensor(oo[:, tb, :].rearrange("p (h d) -> p h d", h=HEADS), o3, bc(rl[:], 2, HD),
                                        ALU.mult).then_inc(oo_ready, 1)
                        after(v, oo_ready, t + 1)
                        v.sem_inc(passed, 1)
                        tl.end()

                    steps(v, NT, tile)

        with ExitStack() as ro:
            wr = sb("wr", [P, 2, X], ctx=ro)
            br = sb("br", [P, X], ctx=ro)
            qrow = sb("qrow", [P, 2, C], ctx=ro)
            qT = sb("qT", [P, 2, C], ctx=ro)
            uT = sb("uT", [P, 2, C], ctx=ro)
            u = sb("u", [P, 2, C], ctx=ro)
            aidx = sb("aidx", [P, 2], I32, ctx=ro)
            arow = sb("arow", [P, 2, C], ctx=ro)
            st = sb("r_st", [P, 2, 6], ctx=ro)
            mv = sb("r_mv", [P, 2, 2], ctx=ro)
            sc = sb("r_sc", [P, 2, 4], ctx=ro)
            lg = sb("lg", [P, X, NT], ctx=ro)
            ex = sb("ex", [P, X, NT], ctx=ro)
            hot1 = sb("hot1", [P, X, NT], ctx=ro)
            hot2 = sb("hot2", [P, X, NT], ctx=ro)
            both = sb("both", [P, X * NT], ctx=ro)
            scan = sb("r_scan", [P, X * NT], ctx=ro)
            small = sb("r_small", [P, 8, NT], ctx=ro)
            best = sb("best", [P, 2, NT], ctx=ro)
            int_a = sb("int_a", [P, X], I32, ctx=ro)
            xstage = sb("xstage", [P, 4, C], ctx=ro)
            pstage = sb("pstage", [P, 4, 2], I32, ctx=ro)
            (ld_wr, c_pool, c_ln, c_dve, c_end, q_copied, q_mm, qt_ready, mix_mm, x2_ready, var_ready, sd_ready, u_ready,
             u_mm, ut_ready, lg_mm, lg_used, var2_ready, sd2_ready, xn_ready) = (
                sem("r_" + s, ro) for s in (
                    "ld_wr", "c_pool", "c_ln", "c_dve", "c_end", "q_copied", "q_mm", "qt_ready", "mix_mm", "x2_ready",
                    "var_ready", "sd_ready", "u_ready", "u_mm", "ut_ready", "lg_mm", "lg_used", "var2_ready",
                    "sd2_ready", "xn_ready"))
            arow_used, cnt_ready, cnt_mm, ex_in, ex_out, place_ready, staged = (
                sem("r_" + s, ro) for s in ("arow_used", "cnt_ready", "cnt_mm", "ex_in", "ex_out", "place_ready", "staged"))
            ld_a = [sem(f"ld_a{i}", ro) for i in range(2)]
            st_x = [sem(f"st_x{i}", ro) for i in range(4)]
            QT, MX, UT, LG = bank[0], bank[1], bank[2], bank[3]

            with nc.Block() as block:
                @block.sync
                def _(sp):
                    sp.dma_start(wr[:], wr_in.rearrange("(o p) c -> p o c", p=P)).then_inc(ld_wr, 16)
                    sp.dma_start(br[:], br_in).then_inc(ld_wr, 16)

                @block.gpsimd
                def _(pool):
                    def fetch(t, b):
                        after(pool, arow_used, t - 1)
                        pool.tensor_copy(aidx[:, b:b + 1], place_i[:, bass.ds(t, 1)]).then_inc(c_pool, 1)
                        gate(pool, c_pool, t + 1, passed)
                        pool.indirect_dma_start(arow[:, b, :], None, aggs,
                                                bass.IndirectOffsetOnAxis(ap=aidx[:, b:b + 1], axis=0)).then_inc(ld_a[b], 16)

                    steps(pool, NT, fetch)

                    def scatter(t, b):
                        gate(pool, staged, 2 * t + 2, passed)
                        for k in range(2):
                            pool.indirect_dma_start(xs, bass.IndirectOffsetOnAxis(ap=pstage[:, b, k:k + 1], axis=0),
                                                    xstage[:, b, :], None).then_inc(st_x[b], 16)

                    steps(pool, NT, scatter, 4)
                    for b in range(4):
                        pool.wait_ge(st_x[b], 32 * (NT // 4 + (b < NT % 4)))

                @block.tensor
                def _(pe):
                    def mix(t, b):
                        after(pe, q_copied, t + 1)
                        after(pe, qt_ready, t)
                        for o in range(2):
                            mm = pe.transpose(QT[:, P * o:P * o + P], qrow[:, b, P * o:P * o + P], ident[:])
                        mm.then_inc(q_mm, 1)
                        after(pe, qt_ready, t + 1)
                        after(pe, x2_ready, t)
                        for o in range(2):
                            mm = pe.matmul(MX[:, 0:C], qT[:, b, P * o:P * o + P], kvo[:, o, :], start=(o == 0), stop=(o == 1))
                        mm.then_inc(mix_mm, 1)

                    def router(t, b):
                        after(pe, u_ready, t + 1)
                        after(pe, ut_ready, t)
                        for o in range(2):
                            mm = pe.transpose(UT[:, P * o:P * o + P], u[:, b, P * o:P * o + P], ident[:])
                        mm.then_inc(u_mm, 1)
                        after(pe, ut_ready, t + 1)
                        after(pe, lg_used, t)
                        for o in range(2):
                            mm = pe.matmul(LG[:, 0:X], uT[:, b, P * o:P * o + P], wr[:, o, :], start=(o == 0), stop=(o == 1))
                        mm.then_inc(lg_mm, 1)

                    def step(t, b):
                        if not (isinstance(t, int) and t == NT):
                            mix(t, b)
                        if not (isinstance(t, int) and t == 0):
                            router(t - 1, 1 - b)

                    pe.wait_ge(ld_wr, 32)
                    steps(pe, NT + 1, step)
                    pe.wait_ge(cnt_ready, 1)
                    pe.matmul(bank[4][:, 0:X], tri[:], small[:, 0, 0:X], start=True, stop=True)
                    pe.matmul(bank[5][:, 0:X], ones[:], small[:, 0, 0:X], start=True, stop=True).then_inc(cnt_mm, 1)

                @block.scalar
                def _(act):
                    def first(t, b):
                        after(act, q_mm, t - 1)
                        act.copy(qrow[:, b, :], at_tile(q2n, t)).then_inc(q_copied, 1)
                        after(act, mix_mm, t - 1)
                        after(act, q_mm, t + 1)
                        act.copy(qT[:, b, :], QT[:, 0:C]).then_inc(qt_ready, 1)
                        after(act, var_ready, t + 1)
                        act.activation(sc[:, b, 0:1], mv[:, b, 1:2], ACT.Sqrt, bias=eps[:, 0:1]).then_inc(sd_ready, 1)
                        after(act, var2_ready, t + 1)
                        act.activation(sc[:, b, 2:3], mv[:, b, 1:2], ACT.Sqrt, bias=eps[:, 0:1]).then_inc(sd2_ready, 1)

                    def second(t, b):
                        after(act, lg_mm, t - 1)
                        after(act, u_mm, t + 1)
                        act.copy(uT[:, b, :], UT[:, 0:C]).then_inc(ut_ready, 1)

                    def step(t, b):
                        if not (isinstance(t, int) and t == NT):
                            first(t, b)
                        if not (isinstance(t, int) and t == 0):
                            second(t - 1, 1 - b)

                    steps(act, NT + 1, step)
                    act.wait_ge(ex_in, 1)
                    act.activation(ex[:], lg[:], ACT.Exp).then_inc(ex_out, 1)

                    def stage(t, b):
                        if isinstance(t, int) and t == 0:
                            act.wait_ge(place_ready, 1)
                        after(act, st_x[b], 8 * (t - b))
                        act.copy(xstage[:, b, :], at_tile(q2n, t)).then_inc(staged, 1)
                        act.copy(pstage[:, b, :], at_tile(xplace, t)).then_inc(staged, 1)

                    steps(act, NT, stage, 4)

                @block.vector
                def _(v):
                    ln = Chain(v, c_ln, 6)

                    def first(t, b):
                        ln.tile(t)
                        row = at_tile(xm, t)
                        after(v, ld_a[b], 8 * (t - b) + 16)
                        v.tensor_tensor(row, row, arow[:, b, :], ALU.add).then_inc(arow_used, 1)
                        after(v, arow_used, t + 1)
                        after(v, mix_mm, t + 1)
                        v.tensor_tensor(row, row, MX[:, 0:C], ALU.add).then_inc(x2_ready, 1)
                        gate(v, x2_ready, t + 1, passed)
                        ln.step(v.bn_stats(st[:, b, :], row))
                        gate(v, c_ln, ln.base + ln.k, passed)
                        v.bn_aggr(mv[:, b, :], st[:, b, :]).then_inc(var_ready, 1)
                        after(v, sd_ready, t + 1)
                        ln.run(v.reciprocal(sc[:, b, 1:2], sc[:, b, 0:1]))
                        after(v, u_mm, t - 1)
                        ln.run(v.tensor_scalar(u[:, b, :], row, mv[:, b, 0:1], sc[:, b, 1:2], ALU.subtract, ALU.mult))
                        v.sem_inc(u_ready, 1)
                        ln.step(v.bn_stats(st[:, b, :], u[:, b, :]))
                        gate(v, c_ln, ln.base + ln.k, passed)
                        v.bn_aggr(mv[:, b, :], st[:, b, :]).then_inc(var2_ready, 1)
                        after(v, sd2_ready, t + 1)
                        ln.run(v.reciprocal(sc[:, b, 3:4], sc[:, b, 2:3]))
                        ln.step(v.tensor_scalar(at_tile(q2n, t), u[:, b, :], mv[:, b, 0:1], sc[:, b, 3:4], ALU.subtract, ALU.mult))
                        ln.end()

                    def second(t, b):
                        after(v, lg_mm, t + 1)
                        v.tensor_tensor(lg[:, :, bass.ds(t, 1)].rearrange("p c a -> p (c a)"), LG[:, 0:X], br[:],
                                        ALU.add).then_inc(lg_used, 1)

                    def step(t, b):
                        if not (isinstance(t, int) and t == NT):
                            first(t, b)
                        if not (isinstance(t, int) and t == 0):
                            second(t - 1, 1 - b)

                    v.wait_ge(ld_wr, 32)
                    steps(v, NT + 1, step)
                    v.wait_ge(lg_used, NT)
                    ch = Chain(v, c_end)
                    top, tmp = small[:, 1, :], small[:, 2, :]

                    def over(a):
                        return a.rearrange("p c t -> p t c")

                    lgv, exv = lg[:], ex[:]
                    ch.run(v.tensor_reduce(top, over(lgv), AX.X, ALU.max))
                    ch.run(v.tensor_tensor(lgv, lgv, bc(top, 1, X), ALU.subtract))
                    v.sem_inc(ex_in, 1)
                    v.wait_ge(ex_out, 1)
                    ch.run(v.tensor_reduce(top, over(exv), AX.X, ALU.add))
                    ch.run(v.reciprocal(tmp, top))
                    ch.run(v.tensor_tensor(lgv, exv, bc(tmp, 1, X), ALU.mult))
                    rank = bc(iota[:, 0:X], 2, NT)
                    for k, hot in enumerate((hot1, hot2)):
                        ch.run(v.tensor_reduce(best[:, k, :], over(lgv), AX.X, ALU.max))
                        ch.run(v.tensor_tensor(exv, lgv, bc(best[:, k, :], 1, X), ALU.is_lt))
                        ch.run(v.scalar_tensor_tensor(out=exv, in0=exv, scalar=float(X), in1=rank, op0=ALU.mult, op1=ALU.add))
                        ch.run(v.tensor_reduce(tmp, over(exv), AX.X, ALU.min))
                        ch.run(v.tensor_tensor(hot[:], rank, bc(tmp, 1, X), ALU.is_equal))
                        if k == 0:
                            ch.run(v.scalar_tensor_tensor(out=lgv, in0=hot[:], scalar=-2.0, in1=lgv, op0=ALU.mult, op1=ALU.add))
                    ch.run(v.tensor_tensor(tmp, best[:, 0, :], best[:, 1, :], ALU.add))
                    ch.run(v.reciprocal(tmp, tmp))
                    for k in range(2):
                        ch.step(v.tensor_tensor(xweight[:, k, :], best[:, k, :], tmp, ALU.mult))
                    b3 = both[:].rearrange("p (c t) -> p c t", c=X)
                    ch.run(v.tensor_tensor(b3, hot1[:], hot2[:], ALU.add))
                    ch.run(v.tensor_reduce(small[:, 0, 0:X], b3, AX.X, ALU.add))
                    v.sem_inc(cnt_ready, 1)

                    def pad(tot):
                        ch.run(v.tensor_scalar(tot, tot, float(FT - 1), float(FT), ALU.add, ALU.max))
                        ch.run(v.tensor_copy(int_a[:], tot))
                        ch.run(v.tensor_scalar(int_a[:], int_a[:], 8, None, ALU.logical_shift_right))
                        ch.run(v.tensor_copy(xinfo[:, 0:X, 0], int_a[:]))
                        ch.run(v.tensor_copy(tot, int_a[:]))
                        ch.run(v.tensor_tensor_scan(small[:, 3, 0:X], ones[:, 0:X], tot, 0.0, ALU.mult, ALU.add))
                        ch.run(v.tensor_copy(xinfo[:, X, 0:1], small[:, 3, X - 1:X]))
                        ch.run(v.tensor_tensor(small[:, 3, 0:X], small[:, 3, 0:X], tot, ALU.subtract))
                        ch.run(v.tensor_copy(xinfo[:, 0:X, 1], small[:, 3, 0:X]))
                        ch.run(v.tensor_scalar(tot, tot, float(FT), None, ALU.mult))

                    places(v, ch, cnt_mm, both, scan, small, bank[4], bank[5], ones, X, pad)
                    s3 = scan[:].rearrange("p (c t) -> p c t", c=X)
                    for k, hot in enumerate((hot1, hot2)):
                        ch.run(v.tensor_tensor(hot[:], hot[:], s3, ALU.mult))
                        ch.run(v.tensor_reduce(tmp, over(hot[:]), AX.X, ALU.add))
                        ch.run(v.tensor_copy(xplace[:, :, k], tmp))
                    v.sem_inc(place_ready, 1)

        with ExitStack() as ff:
            fw1 = sb("fw1", [P, 2, 2, FH], ctx=ff)
            fw2 = sb("fw2", [P, 2, FH // P, C], ctx=ff)
            fb1 = sb("fb1", [P, X * FH // P], ctx=ff)
            fb2 = sb("fb2", [P, X, C], ctx=ff)
            lng = sb("lng", [P, 2 * X], ctx=ff)
            lnb = sb("lnb", [P, 2 * X], ctx=ff)
            xr = sb("xr", [P, 2, C], ctx=ff)
            xT = sb("f_xT", [P, 2, FT], ctx=ff)
            hT = sb("hT", [P, FH // P, FT], ctx=ff)
            yo = sb("yo", [P, 2, C], ctx=ff)
            ld_b, ld_xr, x_mm, xt_ready, h_mm, gelu_done, y_mm, y_out, y_stored, st_y, w_used, y_free, y_rows = (
                sem("f_" + s, ff) for s in ("ld_b", "ld_xr", "x_mm", "xt_ready", "h_mm", "gelu_done", "y_mm", "y_out",
                                            "y_stored", "st_y", "w_used", "y_free", "y_rows"))
            ld_w = [sem(f"f_ld_w{i}", ff) for i in range(2)]
            FM = FH // P
            HB = bank[1:5]

            def tiles_of(eng, e):
                return (eng.value_load(xinfo[0:1, e, 0:1], min_val=1, max_val=FMAX),
                        eng.value_load(xinfo[0:1, e, 1:2], min_val=0, max_val=FMAX))

            with nc.Block() as block:
                @block.sync
                def _(sp):
                    def rows(i):
                        return xs[bass.ds(i * FT, FT), :].rearrange("(r p) c -> p r c", p=P)

                    sp.sem_inc(y_stored, 1)
                    sp.dma_start(xr[:], rows(0)).then_inc(ld_xr, 16)
                    for dst, src in ((fb1[:], b1_in), (fb2[:].rearrange("p e c -> p (e c)"), b2_in), (lng[:], lng_in),
                                     (lnb[:], lnb_in)):
                        sp.dma_start(dst, src).then_inc(ld_b, 16)
                    sp.wait_ge(x_mm, 1)
                    sp.dma_start(xr[:], rows(1)).then_inc(ld_xr, 16)
                    n = sp.value_load(xinfo[0:1, X, 0:1], min_val=1, max_val=FMAX)
                    with sp.Fori(0, n) as i:
                        after(sp, x_mm, i + 2)
                        sp.dma_start(xr[:], rows(i + 2)).then_inc(ld_xr, 16)
                        after(sp, y_out, i + 1)
                        sp.dma_start(ys[bass.ds(i * FT, FT), :].rearrange("(r p) c -> p r c", p=P), yo[:]).then_inc(st_y, 16)
                        after(sp, st_y, (i + 1) * 16)
                        sp.sem_inc(y_stored, 1)
                    after(sp, ld_xr, n * 16 + 32)
                    sp.sem_inc(passed, 1)

                @block.gpsimd
                def _(pool):
                    for e in range(X):
                        after(pool, w_used, e - 1)
                        pool.dma_start(fw1[:, e % 2, :, :], w1[e].rearrange("(o p) f -> p o f", p=P)).then_inc(ld_w[e % 2], 16)
                        pool.dma_start(fw2[:, e % 2, :, :], w2[e].rearrange("(m p) c -> p m c", p=P)).then_inc(ld_w[e % 2], 16)

                @block.tensor
                def _(pe):
                    def turn(i):
                        after(pe, ld_xr, (i + 1) * 16)
                        for o in range(2):
                            for r in range(2):
                                mm = pe.transpose(bank[0][:, FT * o + P * r:FT * o + P * r + P], xr[:, r, P * o:P * o + P], ident[:])
                        mm.then_inc(x_mm, 1)

                    turn(0)
                    for e in range(X):
                        n, before = tiles_of(pe, e)
                        pe.wait_ge(ld_w[e % 2], 32 * (e // 2 + 1))
                        with pe.Fori(0, n) as c:
                            i = pe.snap(before + c)
                            after(pe, xt_ready, i + 1)
                            for m in range(FM):
                                after(pe, gelu_done, i * FM + m + 1)
                                for o in range(2):
                                    mm = pe.matmul(HB[m % 4][:, 0:FT], fw1[:, e % 2, o, P * m:P * m + P], xT[:, o, :],
                                                   start=(o == 0), stop=(o == 1))
                                mm.then_inc(h_mm, 1)
                            turn(i + 1)
                            for r in range(2):
                                if r == 0:
                                    after(pe, y_free, i + 1)
                                for m in range(FM):
                                    if r == 0:
                                        after(pe, gelu_done, i * FM + m + 5)
                                    mm = pe.matmul(bank[5 + r][:, 0:C], hT[:, m, P * r:P * r + P], fw2[:, e % 2, m, :],
                                                   start=(m == 0), stop=(m == FM - 1))
                                mm.then_inc(y_mm, 1)
                        pe.drain().then_inc(w_used, 1)

                @block.scalar
                def _(act):
                    act.sem_inc(gelu_done, 4)
                    act.wait_ge(ld_b, 64)
                    for e in range(X):
                        n, before = tiles_of(act, e)
                        with act.Fori(0, n) as c:
                            i = act.snap(before + c)
                            for m in range(FM):
                                after(act, h_mm, i * FM + m + 1)
                                act.activation(hT[:, m, :], HB[m % 4][:, 0:FT], ACT.Gelu,
                                               bias=fb1[:, FM * e + m:FM * e + m + 1]).then_inc(gelu_done, 1)

                @block.vector
                def _(v):
                    v.sem_inc(y_free, 1)

                    def evac(e):
                        for o in range(2):
                            k = 2 * e + o
                            ins = v.tensor_scalar(xT[:, o, :], bank[0][:, FT * o:FT * o + FT], lng[:, k:k + 1], lnb[:, k:k + 1],
                                                  ALU.mult, ALU.add)
                        ins.then_inc(xt_ready, 1)

                    v.wait_ge(ld_b, 64)
                    v.wait_ge(x_mm, 1)
                    evac(0)
                    for e in range(X):
                        n, before = tiles_of(v, e)
                        with v.Fori(0, n) as c:
                            i = v.snap(before + c)
                            after(v, x_mm, i + 2)
                            v.sem_inc(passed, 1)
                            with v.If(c + 1 < n):
                                evac(e)
                            with v.Else():
                                evac(min(e + 1, X - 1))
                            after(v, y_stored, i + 1)
                            for r in range(2):
                                after(v, y_mm, 2 * i + 1 + r)
                                ins = v.tensor_tensor(yo[:, r, :], bank[5 + r][:, 0:C], fb2[:, e, :], ALU.add)
                                ins.then_inc(y_rows, 1)
                            after(v, y_rows, 2 * i + 2)
                            v.sem_inc(y_out, 1)
                            v.sem_inc(y_free, 1)

        with ExitStack() as co:
            R = 4
            cidx = sb("cidx", [P, R, 2], I32, ctx=co)
            yrow = sb("yrow", [P, R, 2, C], ctx=co)
            orow = sb("orow", [P, R, C], ctx=co)
            c_pool, c_dve, o_ready = (sem("o_" + s, co) for s in ("c_pool", "c_dve", "o_ready"))
            ld_y = [sem(f"ld_y{i}", co) for i in range(R)]
            st_o = [sem(f"st_o{i}", co) for i in range(R)]
            with nc.Block() as block:
                @block.gpsimd
                def _(pool):
                    def fetch(t, b):
                        after(pool, o_ready, t - R + 1)
                        pool.tensor_copy(cidx[:, b, :], at_tile(xplace, t)).then_inc(c_pool, 1)
                        gate(pool, c_pool, t + 1, passed)
                        for k in range(2):
                            pool.indirect_dma_start(yrow[:, b, k, :], None, ys,
                                                    bass.IndirectOffsetOnAxis(ap=cidx[:, b, k:k + 1], axis=0)).then_inc(ld_y[b], 16)

                    steps(pool, NT, fetch, R)

                @block.vector
                def _(v):
                    def add(t, b):
                        after(v, ld_y[b], 8 * (t - b) + 32)
                        v.scalar_tensor_tensor(out=orow[:, b, :], in0=yrow[:, b, 0, :], scalar=xweight[:, 0, bass.ds(t, 1)],
                                               in1=at_tile(xm, t), op0=ALU.mult, op1=ALU.add).then_inc(c_dve, 1)
                        after(v, c_dve, t + 1)
                        v.scalar_tensor_tensor(out=orow[:, b, :], in0=yrow[:, b, 1, :], scalar=xweight[:, 1, bass.ds(t, 1)],
                                               in1=orow[:, b, :], op0=ALU.mult, op1=ALU.add).then_inc(o_ready, 1)

                    def step(t, b):
                        after(v, st_o[b], 4 * (t - b))
                        add(t, b)

                    steps(v, NT, step, R)

                @block.sync
                def _(sp):
                    def store(t, b):
                        after(sp, o_ready, t + 1)
                        if isinstance(t, int) and t == NT - 1:
                            sp.dma_start(out[t * P:N, :], orow[0:LAST, b, :]).then_inc(st_o[b], 16)
                        else:
                            sp.dma_start(out[bass.ds(t * P, P), :], orow[:, b, :]).then_inc(st_o[b], 16)

                    steps(sp, NT, store, R)
                    for b in range(R):
                        sp.wait_ge(st_o[b], 16 * (NT // R + (b < NT % R)))


def kernel(**inputs):
    import concourse.bacc as bacc
    from concourse.bass_utils import run_bass_kernel_spmd

    a = {k: np.asarray(v) for k, v in inputs.items()}

    def rows(v):
        return np.ascontiguousarray(np.broadcast_to(v.reshape(1, -1), (P, v.size)))

    def edges(v, fill):
        pad = np.full((EP - E,) + v.shape[1:], fill, v.dtype)
        return np.ascontiguousarray(np.concatenate([v, pad]).reshape((P, EG) + v.shape[1:]))

    qkv, w, wrow = a["L0_mix_W_qkv"], a["L0_gnn_W"], a["L0_gnn_edge_W"]
    scores = np.zeros((C, 2 * HEADS), np.float32)
    for h in range(HEADS):
        scores[HD * h:HD * h + HD, h] = a["L0_gnn_a_src"][h]
        scores[HD * h:HD * h + HD, HEADS + h] = a["L0_gnn_a_dst"][h]
    erow = np.zeros((4, REC, C), np.float32)
    for r in range(27):
        erow[:, r] = wrow[:, r % 3]
    erow[:, 27:30] = a["L0_gnn_edge_b"]
    sel = np.zeros((4, REC, 3), np.float32)
    for r in range(27):
        sel[:, r, r // 9] = 1.0
    for r in range(3):
        sel[:, 27 + r, r] = 1.0
    arrays = {
        "x": a["x"],
        "dst": edges(a["dst"], NP), "src": edges(a["src"], 0), "attr": edges(a["edge_attr_3"], 0.0),
        "wqk": np.ascontiguousarray(qkv[:, :2 * C]), "bqk": rows(a["L0_mix_b_qkv"][:2 * C]),
        "wvT": np.ascontiguousarray(qkv[:, 2 * C:].T), "bv": np.ascontiguousarray(a["L0_mix_b_qkv"][2 * C:].reshape(2, P).T),
        "wout": a["L0_mix_W_out"], "bout": rows(a["L0_mix_b_out"]), "gbias": rows(a["L0_gnn_bias"]),
        "whT": np.ascontiguousarray(w.T), "wh": w, "asd": scores, "erow": erow.reshape(P, C),
        "wr": a["L0_ffn_Wr"], "br": rows(a["L0_ffn_br"]),
        "lng": np.ascontiguousarray(a["L0_ffn_ln_g"].reshape(X * 2, P).T),
        "lnb": np.ascontiguousarray(a["L0_ffn_ln_b"].reshape(X * 2, P).T),
        "w1": a["L0_ffn_W1"], "b1": np.ascontiguousarray(a["L0_ffn_b1"].reshape(X * FH // P, P).T),
        "w2": a["L0_ffn_W2"], "b2": rows(a["L0_ffn_b2"]),
        "ident": np.eye(P, dtype=np.float32), "tri": np.triu(np.ones((P, P), np.float32), 1),
        "sel": sel.reshape(P, 3), "iota": rows(np.arange(P, dtype=np.float32)),
        "node": np.ascontiguousarray(np.arange(NP, dtype=np.int32).reshape(NT, P).T),
    }
    nc = bacc.Bacc("TRN2", target_bir_lowering=False, num_devices=1)
    given = {f"in_{k}": np.ascontiguousarray(v) for k, v in arrays.items()}
    args = [nc.dram_tensor(k, v.shape, mybir.dt.from_np(v.dtype), kind="ExternalInput").ap() for k, v in given.items()]
    out = nc.dram_tensor("out", (N, C), F32, kind="ExternalOutput").ap()
    gps_kernel(nc, *args, out)
    return run_bass_kernel_spmd(nc, [given], core_ids=[0]).results[0]["out"]
```
